# Optimizing a Trainium2 kernel written in Bass

```python
import numpy as np
import jax
import jax.numpy as jnp

def _softmax(x, axis=-1):
    return jax.nn.softmax(x, axis=axis)
def _gelu(x):
    return jax.nn.gelu(x, approximate=True)
def _silu(x):
    return jax.nn.silu(x)
def _sigmoid(x):
    return jax.nn.sigmoid(x)
def _layernorm(x, axis=-1, eps=1e-5):
    m = jnp.mean(x, axis=axis, keepdims=True)
    v = jnp.var(x, axis=axis, keepdims=True)
    return (x - m) / jnp.sqrt(v + eps)
def _scatter_add(tgt, idx, src, axis=0):
    return tgt.at[idx].add(src)
def _segment_sum(src, seg, n):
    return jax.ops.segment_sum(src, seg, n)

kernel_name = 'mk_conv_seq_d1_conv_nchw1024_ef418f'

def setup_inputs(seed: int = 0):
    np.random.seed(seed)
    _w = jnp.asarray
    def _rec_inputs():
        import jax
        import jax.numpy as jnp
        _gk = jax.random.key(seed)
        x = -0.0002091 + 1 * jax.random.normal(jax.random.fold_in(_gk, 1), (128, 1024, 14, 14), jnp.float32)
        return x
    x = _rec_inputs()
    def _L0_conv_setup():
        import jax, jax.numpy as jnp
        import numpy as np
        from jax import lax
        T = 8

        def _dwconv_t(z, w, b):
            k = w.shape[2]
            p = (k - 1) // 2
            out = lax.conv_general_dilated(z, w, window_strides=(1, 1), padding=[(p, p), (0, 0)], feature_group_count=z.shape[1], dimension_numbers=('NCHW', 'OIHW', 'NCHW'))
            return out + b[None, :, None, None]
        key = jax.random.key(seed)
        ks = jax.random.split(key, 13)
        C, IC, H, W, B = (1024, 512, 14, 14, 16)
        s = lambda k, shp, scale: jax.random.normal(k, shp, dtype=jnp.float32) * scale
        return {'x': s(ks[0], (B * T, C, H, W), 1.0), 'w1': s(ks[1], (IC, C, 1, 1), 0.03), 'b1': s(ks[2], (IC,), 0.02), 'wb1': s(ks[3], (IC, 1, 1, 1), 0.3), 'bb1': s(ks[4], (IC,), 0.02), 'wb2': s(ks[5], (IC, 1, 3, 1), 0.3), 'bb2': s(ks[6], (IC,), 0.02), 'wb3': s(ks[7], (IC, 1, 5, 1), 0.3), 'bb3': s(ks[8], (IC,), 0.02), 'wb4': s(ks[9], (IC, 1, 7, 1), 0.3), 'bb4': s(ks[10], (IC,), 0.02), 'w2': s(ks[11], (C, IC, 1, 1), 0.03), 'b2': s(ks[12], (C,), 0.02)}
    _L0_conv_all = _L0_conv_setup()
    _L0_conv_in = {k: v for k, v in _L0_conv_all.items() if k in ('w1', 'b1', 'wb1', 'bb1', 'wb2', 'bb2', 'wb3', 'bb3', 'wb4', 'bb4', 'w2', 'b2', )}
    del _L0_conv_all

    return {
        "x": x,
        "L0_conv_w1": _L0_conv_in["w1"],
        "L0_conv_b1": _L0_conv_in["b1"],
        "L0_conv_wb1": _L0_conv_in["wb1"],
        "L0_conv_bb1": _L0_conv_in["bb1"],
        "L0_conv_wb2": _L0_conv_in["wb2"],
        "L0_conv_bb2": _L0_conv_in["bb2"],
        "L0_conv_wb3": _L0_conv_in["wb3"],
        "L0_conv_bb3": _L0_conv_in["bb3"],
        "L0_conv_wb4": _L0_conv_in["wb4"],
        "L0_conv_bb4": _L0_conv_in["bb4"],
        "L0_conv_w2": _L0_conv_in["w2"],
        "L0_conv_b2": _L0_conv_in["b2"],
    }

def reference(x, L0_conv_w1, L0_conv_b1, L0_conv_wb1, L0_conv_bb1, L0_conv_wb2, L0_conv_bb2, L0_conv_wb3, L0_conv_bb3, L0_conv_wb4, L0_conv_bb4, L0_conv_w2, L0_conv_b2):
    import jax
    import jax.numpy as jnp
    def _L0_conv_ref(x, w1, b1, wb1, bb1, wb2, bb2, wb3, bb3, wb4, bb4, w2, b2):
        import jax, jax.numpy as jnp
        import numpy as np
        from jax import lax
        T = 8

        def _dwconv_t(z, w, b):
            k = w.shape[2]
            p = (k - 1) // 2
            out = lax.conv_general_dilated(z, w, window_strides=(1, 1), padding=[(p, p), (0, 0)], feature_group_count=z.shape[1], dimension_numbers=('NCHW', 'OIHW', 'NCHW'))
            return out + b[None, :, None, None]
        BT, C, H, W = x.shape
        B = BT // T
        IC = w1.shape[0]
        y = jnp.einsum('nchw,oc->nohw', x, w1[:, :, 0, 0]) + b1[None, :, None, None]
        z = y.reshape(B, T, IC, H, W).transpose(0, 3, 4, 2, 1).reshape(B * H * W, IC, T, 1)
        out = _dwconv_t(z, wb1, bb1) + _dwconv_t(z, wb2, bb2) + _dwconv_t(z, wb3, bb3) + _dwconv_t(z, wb4, bb4)
        out = out.reshape(B, H, W, IC, T).transpose(0, 4, 3, 1, 2).reshape(BT, IC, H, W)
        out = jnp.einsum('nihw,oi->nohw', out, w2[:, :, 0, 0]) + b2[None, :, None, None]
        return x + out

    def _gn(v, G=32, eps=1e-5):
        B_, C_, H_, W_ = v.shape
        g = v.reshape(B_, G, C_ // G, H_, W_)
        m = jnp.mean(g, axis=(2, 3, 4), keepdims=True)
        s = jnp.var(g, axis=(2, 3, 4), keepdims=True)
        return ((g - m) / jnp.sqrt(s + eps)).reshape(v.shape)

    def _ln_c(v, eps=1e-6):
        m = jnp.mean(v, axis=1, keepdims=True)
        s = jnp.var(v, axis=1, keepdims=True)
        return (v - m) / jnp.sqrt(s + eps)

    def _ln_t(v, eps=1e-5):
        m = jnp.mean(v, axis=-1, keepdims=True)
        s = jnp.var(v, axis=-1, keepdims=True)
        return (v - m) / jnp.sqrt(s + eps)

    def _to_tokens(v):
        B_, C_, H_, W_ = v.shape
        return v.reshape(B_, C_, H_ * W_).transpose(0, 2, 1)
    def _from_tokens(t, like):
        B_, C_, H_, W_ = like.shape
        return t.transpose(0, 2, 1).reshape(B_, C_, H_, W_)

    x = _L0_conv_ref(x, L0_conv_w1, L0_conv_b1, L0_conv_wb1, L0_conv_bb1, L0_conv_wb2, L0_conv_bb2, L0_conv_wb3, L0_conv_bb3, L0_conv_wb4, L0_conv_bb4, L0_conv_w2, L0_conv_b2)
    return x


_drawn_inputs = setup_inputs


def setup_inputs(seed=0):
    import zlib

    import numpy as np

    out = dict(_drawn_inputs(seed))
    spreads = {}
    factors = {'L0_conv_b1': 4.876,
     'L0_conv_bb1': 5.318,
     'L0_conv_bb2': 4.973,
     'L0_conv_bb3': 5.279,
     'L0_conv_bb4': 5.004,
     'L0_conv_b2': 3.561}
    for name, (base, spread) in spreads.items():
        noise = np.random.default_rng([zlib.crc32(name.encode()), seed]).standard_normal(out[name].shape)
        drawn = base * np.exp(spread * noise) if base else spread * noise
        out[name] = jnp.asarray(drawn.astype(out[name].dtype))
    for name, factor in factors.items():
        out[name] = (out[name] * factor).astype(out[name].dtype)
    return out
```

```python
from contextlib import ExitStack

import concourse.bass as bass
from concourse import mybir

P = 128


def bottleneck_kernel(nc, x, w1, b1, wb1, bb1, wb2, bb2, wb3, bb3, wb4, bb4, w2, b2, out):
    f32, f32r = mybir.dt.float32, mybir.dt.float32r
    ALU, ACT = mybir.AluOpType, mybir.ActivationFunctionType
    ds = bass.ds

    T = 8
    FRAMES, C, H, W = x.shape
    HID = w1.shape[0]
    HW = H * W
    CLIPS = FRAMES // T
    KB = C // P
    MB = HID // P
    PARTS = 4
    QUARTER = HW // PARTS
    COLS = T * QUARTER
    UNITS = CLIPS * PARTS
    PAIRS = KB // 2
    TAPS = wb4.shape[2]
    MID = TAPS // 2
    SIDE_TAPS = [MID + d for n in range(1, MID + 1) for d in (-n, n)]
    NT = 1 + len(SIDE_TAPS)
    WG = 8

    x_v = x.rearrange("(b t) (p k) h w -> b p t k (h w)", t=T, k=KB)
    out_v = out.rearrange("(b t) (p k) h w -> b p t k (h w)", t=T, k=KB)
    w1_v = w1.rearrange("(p m) c a b -> p m (c a b)", m=MB)
    w2_v = w2.rearrange("(p k) i a b -> p k (i a b)", k=KB)

    ctx = ExitStack()
    with ctx:
        def sb(name, shape, dt=f32):
            return ctx.enter_context(nc.sbuf_tensor(name, shape, dt))

        def sem(name):
            return ctx.enter_context(nc.semaphore(name))

        clips = sb("clips", [P, 2, T, KB, HW])
        w1_hi = sb("w1_hi", [P, KB, MB, P], f32r)
        w1_lo = sb("w1_lo", [P, KB, MB, P], f32r)
        w2_hi = sb("w2_hi", [P, MB, KB, P], f32r)
        w2_lo = sb("w2_lo", [P, MB, KB, P], f32r)
        x_hi = sb("x_hi", [P, KB, COLS], f32r)
        x_lo = sb("x_lo", [P, KB, COLS], f32r)
        d_hi = sb("d_hi", [P, MB, COLS], f32r)
        d_lo = sb("d_lo", [P, MB, COLS], f32r)
        yd = sb("yd", [P, MB + 1, COLS])
        b1_t = sb("b1_t", [P, MB])
        b2_t = sb("b2_t", [P, KB])
        tap1 = sb("tap1", [P, MB, wb1.shape[2]])
        tap2 = sb("tap2", [P, MB, wb2.shape[2]])
        tap3 = sb("tap3", [P, MB, wb3.shape[2]])
        taps = sb("taps", [P, MB, TAPS])
        bbs = sb("bbs", [P, 4, MB])
        bias = sb("bias", [P, MB])

        stage = clips[:, 1, :, :, :].rearrange("p t k s -> p (t k s)")
        w1_raw = stage[:, 0:MB * C].rearrange("p (m c) -> p m c", m=MB)
        w2_raw = stage[:, MB * C:MB * C + KB * HID].rearrange("p (k i) -> p k i", k=KB)
        ident = stage[:, MB * C + KB * HID:MB * C + KB * HID + P]

        y_ps = [ctx.enter_context(nc.psum_tensor(f"y_ps{m}", [P, 512], f32)) for m in range(MB)]
        o_ps = [ctx.enter_context(nc.psum_tensor(f"o_ps{n}", [P, 512], f32)) for n in range(4)]
        OB = len(o_ps)

        w1_loaded = [sem(f"w1_loaded{m}") for m in range(MB)]
        w2_loaded = sem("w2_loaded")
        params_loaded = sem("params_loaded")
        x_loaded = [sem(f"x_loaded{j}") for j in range(PAIRS)]
        out_stored = [sem(f"out_stored{j}") for j in range(PAIRS)]
        pool_step = sem("pool_step")
        ident_ready = sem("ident_ready")
        params_ready = sem("params_ready")
        w_transposed = sem("w_transposed")
        w_hi_ready = sem("w_hi_ready")
        x_hi_ready = sem("x_hi_ready")
        x_lo_ready = sem("x_lo_ready")
        x_pair_used = sem("x_pair_used")
        y_done = sem("y_done")
        y_copied = sem("y_copied")
        tap_done = sem("tap_done")
        d_hi_ready = sem("d_hi_ready")
        d_lo_ready = sem("d_lo_ready")
        o_done = sem("o_done")
        o_read = sem("o_read")

        def group_of(g):
            if g < WG:
                k = g
                return [w1_raw[:, m, k::KB] for m in range(MB)], w1_hi[:, k, :, :], w1_lo[:, k, :, :]
            j, half = divmod(g - WG, 2)
            ks = range(half * 4, half * 4 + 4)
            return ([w2_raw[:, k, j::MB] for k in ks], w2_hi[:, j, half * 4:half * 4 + 4, :],
                    w2_lo[:, j, half * 4:half * 4 + 4, :])

        def unit_x(v, k0, k1):
            slot, part = (v // PARTS) % 2, v % PARTS
            if isinstance(v, int):
                a = clips[:, slot, :, k0:k1, part * QUARTER:(part + 1) * QUARTER]
            else:
                a = clips[:, ds(slot, 1), :, k0:k1, ds(part * QUARTER, QUARTER)]
                a = a.rearrange("p o t k s -> p (o t) k s")
            return a.rearrange("p t k s -> p k t s")

        block = ctx.enter_context(nc.Block())

        @block.sync
        def _(sp):
            for m in range(MB):
                sp.dma_start(w1_raw[:, m, :], w1_v[:, m, :]).then_inc(w1_loaded[m], 16)
            for j in range(PAIRS):
                sp.dma_start(clips[:, 0, :, 2 * j:2 * j + 2, :],
                             x_v[0, :, :, 2 * j:2 * j + 2, :]).then_inc(x_loaded[j], 16)
            sp.dma_start(w2_raw, w2_v).then_inc(w2_loaded, 16)
            sp.wait_ge(w_transposed, 2 * WG)
            for j in range(PAIRS):
                sp.dma_start(clips[:, 1, :, 2 * j:2 * j + 2, :],
                             x_v[1, :, :, 2 * j:2 * j + 2, :]).then_inc(x_loaded[j], 16)

            def store(b, j):
                sp.wait_ge(o_read, 2 * WG + KB * (PARTS - 1) + 2 * (j + 1) + KB * PARTS * b)
                if isinstance(b, int):
                    dst, src = out_v[b], clips[:, b % 2, :, 2 * j:2 * j + 2, :]
                    dst = dst[:, :, 2 * j:2 * j + 2, :]
                else:
                    dst = out_v[ds(b, 1), :, :, 2 * j:2 * j + 2, :].rearrange("o p t k s -> (o p) t k s")
                    src = clips[:, ds(b % 2, 1), :, 2 * j:2 * j + 2, :].rearrange("p o t k s -> p (o t) k s")
                sp.dma_start(dst, src).then_inc(out_stored[j], 16)

            with sp.Fori(0, CLIPS - 2) as b:
                for j in range(PAIRS):
                    store(b, j)
                for j in range(PAIRS):
                    sp.wait_ge(out_stored[j], 16 * b + 16)
                    sp.dma_start(
                        clips[:, ds(b % 2, 1), :, 2 * j:2 * j + 2, :].rearrange("p o t k s -> p (o t) k s"),
                        x_v[ds(b + 2, 1), :, :, 2 * j:2 * j + 2, :].rearrange("o p t k s -> (o p) t k s"),
                    ).then_inc(x_loaded[j], 16)
            for b in (CLIPS - 2, CLIPS - 1):
                for j in range(PAIRS):
                    store(b, j)
            for j in range(PAIRS):
                sp.wait_ge(out_stored[j], 16 * CLIPS)

        @block.gpsimd
        def _(pool):
            nc.gpsimd.memset(ident, 0.0).then_inc(pool_step, 1)
            pool.wait_ge(pool_step, 1)
            nc.gpsimd.affine_select(out=ident, in_=ident, compare_op=ALU.not_equal, fill=1.0, base=0,
                                    pattern=[[-1, P]], channel_multiplier=1).then_inc(ident_ready, 1)
            pool.wait_ge(params_loaded, 16 * 10)
            n = 1
            for t in (tap3, tap2, tap1):
                half = t.shape[2] // 2
                mid = taps[:, :, MID - half:MID + half + 1]
                nc.gpsimd.tensor_tensor(mid, mid, t[:, :, :], ALU.add).then_inc(pool_step, 1)
                n += 1
                pool.wait_ge(pool_step, n)
            nc.gpsimd.tensor_tensor(bias[:, :], bbs[:, 0, :], bbs[:, 1, :], ALU.add).then_inc(pool_step, 1)
            pool.wait_ge(pool_step, n + 1)
            nc.gpsimd.tensor_tensor(bias[:, :], bias[:, :], bbs[:, 2, :], ALU.add).then_inc(pool_step, 1)
            pool.wait_ge(pool_step, n + 2)
            nc.gpsimd.tensor_tensor(bias[:, :], bias[:, :], bbs[:, 3, :], ALU.add).then_inc(params_ready, 1)

        @block.tensor
        def _(pe):
            def transpose_group(g):
                if g == 0:
                    pe.wait_ge(ident_ready, 1)
                if g == WG:
                    pe.wait_ge(w2_loaded, 16)
                if g >= OB:
                    pe.wait_ge(o_read, g - OB + 1)
                blocks, _, _ = group_of(g)
                for n, w in enumerate(blocks):
                    if g == 0:
                        pe.wait_ge(w1_loaded[n], 16)
                    last = nc.tensor.transpose(o_ps[g % OB][:, n * P:(n + 1) * P], w, ident)
                last.then_inc(w_transposed, 1)

            def conv1(v, first=False):
                for k in range(KB):
                    if first:
                        pe.wait_ge(o_read, k + 1)
                    if k % 2 == 0:
                        pe.wait_ge(x_lo_ready, PAIRS * v + (k // 2 + 1))
                    for m in range(MB):
                        if k == 0 and not first:
                            pe.wait_ge(y_copied, MB * v + (m + 1 - MB))
                        hi, lo = w1_hi[:, k, m, :], w1_lo[:, k, m, :]
                        y = y_ps[m][:, 0:COLS]
                        nc.tensor.matmul(y, hi, x_hi[:, k, :], start=(k == 0), stop=False)
                        nc.tensor.matmul(y, hi, x_lo[:, k, :], start=False, stop=False)
                        last = nc.tensor.matmul(y, lo, x_hi[:, k, :], start=False, stop=(k == KB - 1))
                        if k == KB - 1:
                            last.then_inc(y_done, 1)
                        elif k % 2 == 1 and m == MB - 1:
                            last.then_inc(x_pair_used, 1)

            def conv2(v):
                pe.wait_ge(d_lo_ready, MB * v + MB)
                for k in range(KB):
                    pe.wait_ge(o_read, 2 * WG + k + 1 - OB + KB * v)
                    o = o_ps[k % OB][:, 0:COLS]
                    for j in range(MB):
                        hi, lo = w2_hi[:, j, k, :], w2_lo[:, j, k, :]
                        nc.tensor.matmul(o, hi, d_hi[:, j, :], start=(j == 0), stop=False)
                        nc.tensor.matmul(o, hi, d_lo[:, j, :], start=False, stop=False)
                        last = nc.tensor.matmul(o, lo, d_hi[:, j, :], start=False, stop=(j == MB - 1))
                    last.then_inc(o_done, 1)

            for g in range(WG):
                transpose_group(g)
            conv1(0, first=True)
            for g in range(WG, 2 * WG):
                transpose_group(g)
            pe.wait_ge(o_read, 2 * WG)
            with pe.Fori(0, UNITS - 1) as u:
                conv1(u + 1)
                conv2(u)
            conv2(UNITS - 1)

        @block.scalar
        def _(act):
            for dst, src in ((taps[:, :, :], wb4), (tap3[:, :, :], wb3), (tap2[:, :, :], wb2),
                             (tap1[:, :, :], wb1)):
                act.dma_start(dst, src.rearrange("(p m) a t b -> p m (a t b)", m=MB)).then_inc(params_loaded, 16)
            for dst, src in ((bbs[:, 0, :], bb1), (bbs[:, 1, :], bb2), (bbs[:, 2, :], bb3),
                             (bbs[:, 3, :], bb4), (b1_t[:, :], b1), (b2_t[:, :], b2)):
                act.dma_start(dst, src.rearrange("(p m) -> p m", p=P)).then_inc(params_loaded, 16)

            def weights_hi(g):
                act.wait_ge(w_transposed, g + 1)
                _, hi, _ = group_of(g)
                src = o_ps[g % OB][:, :].rearrange("p (n c) -> p n c", c=P)
                nc.scalar.activation(hi, src, ACT.Copy).then_inc(w_hi_ready, 1)

            def split_x(v, j, first=False):
                act.wait_ge(x_loaded[j], 16 * (v // PARTS) + 16)
                if not first:
                    if j < PAIRS - 1:
                        act.wait_ge(x_pair_used, (PAIRS - 1) * v + (j + 1 - (PAIRS - 1)))
                    else:
                        act.wait_ge(y_done, MB * v)
                dst = x_hi[:, 2 * j:2 * j + 2, :].rearrange("p k (t s) -> p k t s", t=T)
                nc.scalar.activation(dst, unit_x(v, 2 * j, 2 * j + 2), ACT.Copy).then_inc(x_hi_ready, 1)

            def copy_y(v, m, first=False):
                act.wait_ge(y_done, MB * v + (m + 1))
                if not first:
                    act.wait_ge(d_lo_ready, MB * v)
                nc.scalar.activation(yd[:, m, :], y_ps[m][:, 0:COLS], ACT.Identity,
                                     bias=b1_t[:, m:m + 1]).then_inc(y_copied, 1)

            def split_d(v, m, first=False):
                act.wait_ge(tap_done, NT * MB * v + NT * (m + 1))
                if not first and m == 0:
                    act.wait_ge(o_done, KB * v)
                nc.scalar.activation(d_hi[:, m, :], yd[:, (m - 1) % (MB + 1), :], ACT.Copy).then_inc(d_hi_ready, 1)

            for g in range(WG):
                weights_hi(g)
            for j in range(PAIRS):
                split_x(0, j, first=True)
            for g in range(WG, 2 * WG):
                weights_hi(g)
            for j in range(PAIRS):
                split_x(1, j)
            act.wait_ge(params_ready, 1)
            for m in range(MB):
                copy_y(0, m, first=True)
            def beside(u, first=False, x_too=True):
                for m in range(MB):
                    split_d(u, m, first)
                if x_too:
                    for j in range(PAIRS - 1):
                        split_x(u + 2, j)
                for m in range(MB):
                    copy_y(u + 1, m)
                if x_too:
                    split_x(u + 2, PAIRS - 1)

            beside(0, first=True)
            with act.Fori(1, UNITS - 2) as u:
                beside(u)
            beside(UNITS - 2, x_too=False)
            for m in range(MB):
                split_d(UNITS - 1, m)

        @block.vector
        def _(dve):
            def weights_lo(g):
                dve.wait_ge(w_hi_ready, g + 1)
                _, hi, lo = group_of(g)
                src = o_ps[g % OB][:, :].rearrange("p (n c) -> p n c", c=P)
                nc.vector.tensor_tensor(lo, src, hi.bitcast(f32), ALU.subtract).then_inc(o_read, 1)

            def split_x(v, j):
                dve.wait_ge(x_hi_ready, PAIRS * v + (j + 1))
                hi = x_hi[:, 2 * j:2 * j + 2, :].bitcast(f32).rearrange("p k (t s) -> p k t s", t=T)
                lo = x_lo[:, 2 * j:2 * j + 2, :].rearrange("p k (t s) -> p k t s", t=T)
                nc.vector.tensor_tensor(lo, unit_x(v, 2 * j, 2 * j + 2), hi, ALU.subtract).then_inc(x_lo_ready, 1)

            def depthwise(v, m):
                dve.wait_ge(y_copied, MB * v + (m + 1))
                if m > 0:
                    dve.wait_ge(tap_done, NT * MB * v + NT * m)
                d, y = yd[:, (m - 1) % (MB + 1), :], yd[:, m, :]
                nc.vector.tensor_scalar(d, y, taps[:, m, MID:MID + 1], bias[:, m:m + 1],
                                        ALU.mult, ALU.add).then_inc(tap_done, 1)
                for n, tap in enumerate(SIDE_TAPS):
                    shift = (tap - MID) * QUARTER
                    to = slice(max(0, -shift), COLS - max(0, shift))
                    of = slice(max(0, shift), COLS - max(0, -shift))
                    dve.wait_ge(tap_done, NT * MB * v + (NT * m + n + 1))
                    nc.vector.scalar_tensor_tensor(d[:, to], y[:, of], taps[:, m, tap:tap + 1], d[:, to],
                                                   ALU.mult, ALU.add).then_inc(tap_done, 1)

            def split_d(v, m):
                dve.wait_ge(d_hi_ready, MB * v + (m + 1))
                nc.vector.tensor_tensor(d_lo[:, m, :], yd[:, (m - 1) % (MB + 1), :],
                                        d_hi[:, m, :].bitcast(f32), ALU.subtract).then_inc(d_lo_ready, 1)

            def add_out(v, k):
                dve.wait_ge(o_done, KB * v + (k + 1))
                xs = unit_x(v, k, k + 1).rearrange("p k t s -> p (k t) s")
                o = o_ps[k % OB][:, 0:COLS].rearrange("p (t s) -> p t s", t=T)
                nc.vector.scalar_tensor_tensor(xs, o, b2_t[:, k:k + 1], xs, ALU.add, ALU.add).then_inc(o_read, 1)

            for g in range(WG):
                weights_lo(g)
            for j in range(PAIRS):
                split_x(0, j)
            for g in range(WG, 2 * WG):
                weights_lo(g)
            for j in range(PAIRS):
                split_x(1, j)
            dve.wait_ge(params_ready, 1)
            for m in range(MB):
                depthwise(0, m)

            def beside(u, x_too=True):
                for m in range(MB):
                    split_d(u, m)
                if x_too:
                    for j in range(PAIRS - 1):
                        split_x(u + 2, j)
                for m in range(MB):
                    depthwise(u + 1, m)
                    for k in range(2 * m, 2 * m + 2):
                        add_out(u, k)
                    if m == 0 and x_too:
                        split_x(u + 2, PAIRS - 1)

            with dve.Fori(0, UNITS - 2) as u:
                beside(u)
            beside(UNITS - 2, x_too=False)
            for m in range(MB):
                split_d(UNITS - 1, m)
            for k in range(KB):
                add_out(UNITS - 1, k)


_INS = ['x', 'L0_conv_w1', 'L0_conv_b1', 'L0_conv_wb1', 'L0_conv_bb1', 'L0_conv_wb2', 'L0_conv_bb2',
        'L0_conv_wb3', 'L0_conv_bb3', 'L0_conv_wb4', 'L0_conv_bb4', 'L0_conv_w2', 'L0_conv_b2']


def kernel(**inputs):
    import numpy as _np
    import concourse.bacc as _bacc
    from concourse import mybir as _mybir
    from concourse.bass_utils import run_bass_kernel_spmd as _run

    nc = _bacc.Bacc("TRN2", target_bir_lowering=False, num_devices=1)
    arrays, args = {}, []
    for name in _INS:
        a = _np.ascontiguousarray(inputs[name])
        arrays[f"in_{name}_dram"] = a
        args.append(nc.dram_tensor(f"in_{name}_dram", a.shape, _mybir.dt.from_np(a.dtype), kind="ExternalInput").ap())
    shape = inputs['x'].shape
    out = nc.dram_tensor("out_dram", shape, _mybir.dt.float32, kind="ExternalOutput").ap()
    bottleneck_kernel(nc, *args, out)
    r = _run(nc, [arrays], core_ids=[0])
    return r.results[0]["out_dram"]
```

```python
from contextlib import ExitStack

import concourse.bass as bass
from concourse import mybir

P = 128


def bottleneck_kernel(nc, x, w1, w2, small, small_sizes, out):
    f32, f32r = mybir.dt.float32, mybir.dt.float32r
    ALU, ACT = mybir.AluOpType, mybir.ActivationFunctionType
    ds = bass.ds

    T = 8
    FRAMES, C, H, W = x.shape
    HID = w1.shape[2] * P
    HW = H * W
    CLIPS = FRAMES // T
    KB = C // P
    MB = HID // P
    PARTS = 4
    QUARTER = HW // PARTS
    COLS = T * QUARTER
    UNITS = CLIPS * PARTS
    PAIRS = KB // 2
    TAPS = small_sizes['wb4'] // MB
    MID = TAPS // 2
    SIDE_TAPS = [MID + d for n in range(1, MID + 1) for d in (-n, n)]
    NT = 1 + len(SIDE_TAPS)

    x_v = x.rearrange("(b t) (p k) h w -> b p t k (h w)", t=T, k=KB)
    out_v = out.rearrange("(b t) (p k) h w -> b p t k (h w)", t=T, k=KB)

    ctx = ExitStack()
    with ctx:
        def sb(name, shape, dt=f32):
            return ctx.enter_context(nc.sbuf_tensor(name, shape, dt))

        def sem(name):
            return ctx.enter_context(nc.semaphore(name))

        clips = sb("clips", [P, 2, T, KB, HW])
        w1_hi = sb("w1_hi", [P, KB, MB, P], f32r)
        w1_lo = sb("w1_lo", [P, KB, MB, P], f32r)
        w2_hi = sb("w2_hi", [P, MB, KB, P], f32r)
        w2_lo = sb("w2_lo", [P, MB, KB, P], f32r)
        x_hi = sb("x_hi", [P, KB, COLS], f32r)
        x_lo = sb("x_lo", [P, KB, COLS], f32r)
        d_hi = sb("d_hi", [P, MB, COLS], f32r)
        d_lo = sb("d_lo", [P, MB, COLS], f32r)
        yd = sb("yd", [P, MB + 2, COLS])
        D_AT = [(m + MB) % (MB + 2) for m in range(MB)]
        params = sb("params", [P, small.shape[1]])
        bias = sb("bias", [P, MB])

        at, end = {}, 0
        for name, size in small_sizes.items():
            at[name] = params[:, end:end + size]
            end += size
        b1_t, b2_t = at['b1'], at['b2']
        kernels = [at[f'wb{n}'].rearrange("p (m t) -> p m t", m=MB) for n in range(1, 5)]
        taps = kernels[3]

        stage = clips[:, 1, :, :, :].rearrange("p t k s -> p (t k s)")
        w1_raw = stage[:, 0:C * MB].rearrange("p (k m o) -> p k m o", k=KB, m=MB)
        w2_raw = stage[:, C * MB:2 * C * MB].rearrange("p (j k o) -> p j k o", j=MB, k=KB)

        y_ps = [ctx.enter_context(nc.psum_tensor(f"y_ps{m}", [P, 512], f32)) for m in range(MB)]
        o_ps = [ctx.enter_context(nc.psum_tensor(f"o_ps{n}", [P, 512], f32)) for n in range(4)]
        OB = len(o_ps)

        w1_loaded = [sem(f"w1_loaded{k}") for k in range(KB)]
        w2_loaded = [sem(f"w2_loaded{j}") for j in range(MB)]
        params_loaded = sem("params_loaded")
        x_loaded = [sem(f"x_loaded{j}") for j in range(PAIRS)]
        first_loaded = [sem(f"first_loaded{k}") for k in range(KB)]
        out_stored = [sem(f"out_stored{j}") for j in range(PAIRS)]
        last_stored = [sem(f"last_stored{j}") for j in range(PAIRS)]
        pool_step = sem("pool_step")
        params_ready = sem("params_ready")
        first_hi_ready = sem("first_hi_ready")
        first_lo_ready = sem("first_lo_ready")
        w2_hi_ready = sem("w2_hi_ready")
        w2_lo_ready = sem("w2_lo_ready")
        x_hi_ready = sem("x_hi_ready")
        x_lo_ready = sem("x_lo_ready")
        x_pair_used = sem("x_pair_used")
        y_done = sem("y_done")
        y_copied = sem("y_copied")
        tap_done = sem("tap_done")
        d_hi_ready = sem("d_hi_ready")
        d_lo_ready = sem("d_lo_ready")
        o_done = sem("o_done")
        o_read = sem("o_read")

        last_hi, last_lo = x_hi[:, 0:MB, :], x_lo[:, 0:MB, :]

        def unit_x(v, k0, k1):
            slot, part = (v // PARTS) % 2, v % PARTS
            if isinstance(v, int):
                a = clips[:, slot, :, k0:k1, part * QUARTER:(part + 1) * QUARTER]
            else:
                a = clips[:, ds(slot, 1), :, k0:k1, ds(part * QUARTER, QUARTER)]
                a = a.rearrange("p o t k s -> p (o t) k s")
            return a.rearrange("p t k s -> p k t s")

        block = ctx.enter_context(nc.Block())

        @block.sync
        def _(sp):
            for k in range(KB):
                sp.dma_start(w1_raw[:, k, :, :], w1[:, k, :, :]).then_inc(w1_loaded[k], 16)
                sp.dma_start(clips[:, 0, :, k, 0:QUARTER], x_v[0, :, :, k, 0:QUARTER]).then_inc(first_loaded[k], 16)
            for j in range(PAIRS):
                for k in (2 * j, 2 * j + 1):
                    sp.dma_start(clips[:, 0, :, k, QUARTER:HW],
                                 x_v[0, :, :, k, QUARTER:HW]).then_inc(x_loaded[j], 16)
                for i in range(j * MB // PAIRS, (j + 1) * MB // PAIRS):
                    sp.dma_start(w2_raw[:, i, :, :], w2[:, i, :, :]).then_inc(w2_loaded[i], 16)
            sp.wait_ge(first_lo_ready, 2 * KB)
            sp.wait_ge(w2_lo_ready, MB)
            for j in range(PAIRS):
                sp.dma_start(clips[:, 1, :, 2 * j:2 * j + 2, :],
                             x_v[1, :, :, 2 * j:2 * j + 2, :]).then_inc(x_loaded[j], 16)

            def store(b, j):
                sp.wait_ge(o_read, KB * (PARTS - 1) + 2 * (j + 1) + KB * PARTS * b)
                if isinstance(b, int):
                    dst, src = out_v[b][:, :, 2 * j:2 * j + 2, :], clips[:, b % 2, :, 2 * j:2 * j + 2, :]
                else:
                    dst = out_v[ds(b, 1), :, :, 2 * j:2 * j + 2, :].rearrange("o p t k s -> (o p) t k s")
                    src = clips[:, ds(b % 2, 1), :, 2 * j:2 * j + 2, :].rearrange("p o t k s -> p (o t) k s")
                sp.dma_start(dst, src).then_inc(out_stored[j], 16)

            with sp.Fori(0, CLIPS - 2) as b:
                for j in range(PAIRS):
                    store(b, j)
                for j in range(PAIRS):
                    sp.wait_ge(out_stored[j], 16 * b + 16)
                    sp.dma_start(
                        clips[:, ds(b % 2, 1), :, 2 * j:2 * j + 2, :].rearrange("p o t k s -> p (o t) k s"),
                        x_v[ds(b + 2, 1), :, :, 2 * j:2 * j + 2, :].rearrange("o p t k s -> (o p) t k s"),
                    ).then_inc(x_loaded[j], 16)
            for j in range(PAIRS):
                store(CLIPS - 2, j)
            b, rest = CLIPS - 1, HW - QUARTER
            for j in range(PAIRS):
                for k in (2 * j, 2 * j + 1):
                    sp.wait_ge(o_read, KB * (UNITS - 2) + k + 1)
                    sp.dma_start(out_v[b][:, :, k, 0:rest],
                                 clips[:, b % 2, :, k, 0:rest]).then_inc(out_stored[j], 16)
            for j in range(PAIRS):
                for k in (2 * j, 2 * j + 1):
                    sp.wait_ge(o_read, KB * (UNITS - 1) + k + 1)
                    sp.dma_start(out_v[b][:, :, k, rest:HW],
                                 clips[:, b % 2, :, k, rest:HW]).then_inc(last_stored[j], 16)
            for j in range(PAIRS):
                sp.wait_ge(out_stored[j], 16 * (CLIPS + 1))
                sp.wait_ge(last_stored[j], 32)

        @block.gpsimd
        def _(pool):
            pool.wait_ge(params_loaded, 16)
            n = 0
            for t in (kernels[2], kernels[1], kernels[0]):
                half = t.shape[2] // 2
                mid = taps[:, :, MID - half:MID + half + 1]
                nc.gpsimd.tensor_tensor(mid, mid, t, ALU.add).then_inc(pool_step, 1)
                n += 1
                pool.wait_ge(pool_step, n)
            nc.gpsimd.tensor_tensor(bias[:, :], at['bb1'], at['bb2'], ALU.add).then_inc(pool_step, 1)
            pool.wait_ge(pool_step, n + 1)
            nc.gpsimd.tensor_tensor(bias[:, :], bias[:, :], at['bb3'], ALU.add).then_inc(pool_step, 1)
            pool.wait_ge(pool_step, n + 2)
            nc.gpsimd.tensor_tensor(bias[:, :], bias[:, :], at['bb4'], ALU.add).then_inc(params_ready, 1)
            for j in range(MB):
                pool.wait_ge(w2_hi_ready, j + 1)
                nc.gpsimd.tensor_tensor(w2_lo[:, j, :, :], w2_raw[:, j, :, :], w2_hi[:, j, :, :].bitcast(f32),
                                        ALU.subtract).then_inc(w2_lo_ready, 1)

        @block.tensor
        def _(pe):
            def products1(v, k, m):
                hi, lo = w1_hi[:, k, m, :], w1_lo[:, k, m, :]
                y = y_ps[m][:, 0:COLS]
                nc.tensor.matmul(y, hi, x_hi[:, k, :], start=(k == 0), stop=False)
                nc.tensor.matmul(y, hi, x_lo[:, k, :], start=False, stop=False)
                last = nc.tensor.matmul(y, lo, x_hi[:, k, :], start=False, stop=(k == KB - 1))
                if k == KB - 1:
                    last.then_inc(y_done, 1)
                return last

            def conv1(v, first=False):
                for k in range(KB):
                    if first:
                        pe.wait_ge(first_lo_ready, 2 * (k + 1))
                    elif k % 2 == 0:
                        pe.wait_ge(x_lo_ready, PAIRS * v + (k // 2 + 1 - PAIRS))
                    for m in range(MB):
                        if k == 0 and not first:
                            pe.wait_ge(y_copied, MB * v + (m + 1 - MB))
                        last = products1(v, k, m)
                    if k % 2 == 1 and k < KB - 1:
                        last.then_inc(x_pair_used, 1)

            def conv1_last(v):
                for m in range(MB):
                    pe.wait_ge(y_copied, MB * v + (m + 1 - MB))
                    for k in range(KB):
                        if m == 0 and k % 2 == 0:
                            pe.wait_ge(x_lo_ready, PAIRS * v + (k // 2 + 1 - PAIRS))
                        products1(v, k, m)

            def conv2(v, first=False, d_hi=d_hi, d_lo=d_lo):
                for k in range(KB):
                    if not first or k >= OB:
                        pe.wait_ge(o_read, KB * v + (k + 1 - OB))
                    o = o_ps[k % OB][:, 0:COLS]
                    for j in range(MB):
                        if first and k == 0:
                            pe.wait_ge(w2_lo_ready, j + 1)
                        if k == 0:
                            pe.wait_ge(d_lo_ready, MB * v + (j + 1))
                        hi, lo = w2_hi[:, j, k, :], w2_lo[:, j, k, :]
                        nc.tensor.matmul(o, hi, d_hi[:, j, :], start=(j == 0), stop=False)
                        nc.tensor.matmul(o, hi, d_lo[:, j, :], start=False, stop=False)
                        last = nc.tensor.matmul(o, lo, d_hi[:, j, :], start=False, stop=(j == MB - 1))
                    last.then_inc(o_done, 1)

            conv1(0, first=True)
            conv1(1)
            conv2(0, first=True)
            with pe.Fori(1, UNITS - 2) as u:
                conv1(u + 1)
                conv2(u)
            conv1_last(UNITS - 1)
            conv2(UNITS - 2)
            conv2(UNITS - 1, d_hi=last_hi, d_lo=last_lo)

        @block.scalar
        def _(act):
            act.dma_start(params[:, :], small).then_inc(params_loaded, 16)

            def split_first(k):
                act.wait_ge(w1_loaded[k], 16)
                nc.scalar.activation(w1_hi[:, k, :, :], w1_raw[:, k, :, :], ACT.Copy).then_inc(first_hi_ready, 1)
                act.wait_ge(first_loaded[k], 16)
                nc.scalar.activation(x_hi[:, k, :].rearrange("p (t s) -> p t s", t=T),
                                     clips[:, 0, :, k, 0:QUARTER], ACT.Copy).then_inc(first_hi_ready, 1)

            def split_w2(j):
                act.wait_ge(w2_loaded[j], 16)
                nc.scalar.activation(w2_hi[:, j, :, :], w2_raw[:, j, :, :], ACT.Copy).then_inc(w2_hi_ready, 1)

            def split_x(v, j):
                act.wait_ge(x_loaded[j], 16 * (v // PARTS) + 32)
                if j < PAIRS - 1:
                    act.wait_ge(x_pair_used, (PAIRS - 1) * v + (j + 1 - (PAIRS - 1)))
                else:
                    act.wait_ge(y_done, MB * v)
                dst = x_hi[:, 2 * j:2 * j + 2, :].rearrange("p k (t s) -> p k t s", t=T)
                nc.scalar.activation(dst, unit_x(v, 2 * j, 2 * j + 2), ACT.Copy).then_inc(x_hi_ready, 1)

            def copy_y(v, m, first=False):
                act.wait_ge(y_done, MB * v + (m + 1))
                if not first:
                    act.wait_ge(d_lo_ready, MB * v)
                if first and m == 0:
                    act.wait_ge(params_loaded, 16)
                nc.scalar.activation(yd[:, m, :], y_ps[m][:, 0:COLS], ACT.Identity,
                                     bias=b1_t[:, m:m + 1]).then_inc(y_copied, 1)

            def split_d(v, m, first=False, hi=d_hi):
                act.wait_ge(tap_done, NT * MB * v + (NT * (m + 1) if m % 2 else NT * (m + 2) - 1))
                if not first and m == 0:
                    if hi is d_hi:
                        act.wait_ge(o_done, KB * v)
                    else:
                        act.wait_ge(y_done, MB * v + MB)
                nc.scalar.activation(hi[:, m, :], yd[:, D_AT[m], :], ACT.Copy).then_inc(d_hi_ready, 1)

            for k in range(KB):
                split_first(k)
            split_x(1, 0)
            split_w2(0)
            for m in range(MB):
                copy_y(0, m, first=True)
            split_x(1, 1)
            split_w2(1)
            split_x(1, 2)
            split_w2(2)
            split_d(0, 0, first=True)
            split_d(0, 1, first=True)
            split_x(1, 3)
            split_w2(3)
            split_d(0, 2, first=True)
            split_d(0, 3, first=True)
            for j in range(PAIRS - 1):
                split_x(2, j)
            for m in range(MB):
                copy_y(1, m)
            split_x(2, PAIRS - 1)

            with act.Fori(1, UNITS - 2) as u:
                for m in range(MB):
                    split_d(u, m)
                for j in range(PAIRS - 1):
                    split_x(u + 2, j)
                for m in range(MB):
                    copy_y(u + 1, m)
                split_x(u + 2, PAIRS - 1)
            for m in range(MB):
                split_d(UNITS - 2, m)
            for m in range(MB):
                copy_y(UNITS - 1, m)
            for m in range(MB):
                split_d(UNITS - 1, m, hi=last_hi)

        @block.vector
        def _(dve):
            def split_first(k):
                dve.wait_ge(first_hi_ready, 2 * k + 1)
                nc.vector.tensor_tensor(w1_lo[:, k, :, :], w1_raw[:, k, :, :], w1_hi[:, k, :, :].bitcast(f32),
                                        ALU.subtract).then_inc(first_lo_ready, 1)
                dve.wait_ge(first_hi_ready, 2 * k + 2)
                hi, lo = (a.rearrange("p (t s) -> p t s", t=T) for a in (x_hi[:, k, :].bitcast(f32), x_lo[:, k, :]))
                nc.vector.tensor_tensor(lo, clips[:, 0, :, k, 0:QUARTER], hi, ALU.subtract).then_inc(first_lo_ready, 1)

            def split_x(v, j):
                dve.wait_ge(x_hi_ready, PAIRS * v + (j + 1 - PAIRS))
                hi = x_hi[:, 2 * j:2 * j + 2, :].bitcast(f32).rearrange("p k (t s) -> p k t s", t=T)
                lo = x_lo[:, 2 * j:2 * j + 2, :].rearrange("p k (t s) -> p k t s", t=T)
                nc.vector.tensor_tensor(lo, unit_x(v, 2 * j, 2 * j + 2), hi, ALU.subtract).then_inc(x_lo_ready, 1)

            def depthwise(v, m, sums=lambda n: None):
                before = NT * MB * v
                dve.wait_ge(y_copied, MB * v + (m + 2))
                if m > 0:
                    dve.wait_ge(tap_done, before + NT * m)
                for i in (m, m + 1):
                    nc.vector.tensor_scalar(yd[:, D_AT[i], :], yd[:, i, :], taps[:, i, MID:MID + 1],
                                            bias[:, i:i + 1], ALU.mult, ALU.add).then_inc(tap_done, 1)
                sums(0)
                for n, tap in enumerate(SIDE_TAPS):
                    shift = (tap - MID) * QUARTER
                    to = slice(max(0, -shift), COLS - max(0, shift))
                    of = slice(max(0, shift), COLS - max(0, -shift))
                    for i in (m, m + 1):
                        d = yd[:, D_AT[i], to]
                        dve.wait_ge(tap_done, before + (NT * m + 2 * n + 1 + i - m))
                        nc.vector.scalar_tensor_tensor(d, yd[:, i, of], taps[:, i, tap:tap + 1], d,
                                                       ALU.mult, ALU.add).then_inc(tap_done, 1)
                    sums(n + 1)

            def split_d(v, m, hi=d_hi, lo=d_lo):
                dve.wait_ge(d_hi_ready, MB * v + (m + 1))
                nc.vector.tensor_tensor(lo[:, m, :], yd[:, D_AT[m], :],
                                        hi[:, m, :].bitcast(f32), ALU.subtract).then_inc(d_lo_ready, 1)

            def add_out(v, k):
                dve.wait_ge(o_done, KB * v + (k + 1))
                xs = unit_x(v, k, k + 1).rearrange("p k t s -> p (k t) s")
                o = o_ps[k % OB][:, 0:COLS].rearrange("p (t s) -> p t s", t=T)
                nc.vector.scalar_tensor_tensor(xs, o, b2_t[:, k:k + 1], xs, ALU.add, ALU.add).then_inc(o_read, 1)

            for k in range(KB):
                split_first(k)
            split_x(1, 0)
            split_x(1, 1)
            dve.wait_ge(params_ready, 1)
            depthwise(0, 0, lambda n: split_x(1, 2) if n == 4 else None)
            split_d(0, 0)
            split_d(0, 1)
            depthwise(0, 2, lambda n: split_x(1, 3) if n == 1 else None)
            split_d(0, 2)
            split_d(0, 3)
            for j in range(PAIRS - 1):
                split_x(2, j)

            def sums_of(u, m):
                turns = {1: 2 * m, 3: 2 * m + 1, 5: 2 * m + 2, 6: 2 * m + 3}
                return lambda n: add_out(u, turns[n]) if n in turns else None

            def beside_conv2(u):
                depthwise(u + 1, 0, sums_of(u, 0))
                split_x(u + 2, PAIRS - 1)
                depthwise(u + 1, 2, sums_of(u, 2))

            beside_conv2(0)
            with dve.Fori(1, UNITS - 2) as u:
                for m in range(MB):
                    split_d(u, m)
                for j in range(PAIRS - 1):
                    split_x(u + 2, j)
                beside_conv2(u)
            for m in range(MB):
                split_d(UNITS - 2, m)
            depthwise(UNITS - 1, 0)
            split_d(UNITS - 1, 0, last_hi, last_lo)
            split_d(UNITS - 1, 1, last_hi, last_lo)
            depthwise(UNITS - 1, 2, sums_of(UNITS - 2, 0))
            split_d(UNITS - 1, 2, last_hi, last_lo)
            split_d(UNITS - 1, 3, last_hi, last_lo)
            for k in range(KB // 2, KB):
                add_out(UNITS - 2, k)
            for k in range(KB):
                add_out(UNITS - 1, k)


_SMALL = ['b1', 'wb1', 'wb2', 'wb3', 'wb4', 'bb1', 'bb2', 'bb3', 'bb4', 'b2']


def kernel(**inputs):
    import numpy as _np
    import concourse.bacc as _bacc
    from concourse import mybir as _mybir
    from concourse.bass_utils import run_bass_kernel_spmd as _run

    def stationary(w):
        w = _np.asarray(w)
        n_out, n_in = w.shape[:2]
        return w.reshape(P, n_out // P, P, n_in // P).transpose(2, 3, 1, 0)

    rows = {name: _np.asarray(inputs[f'L0_conv_{name}']).reshape(P, -1) for name in _SMALL}
    sizes = {name: a.shape[1] for name, a in rows.items()}
    given = {
        'x': _np.asarray(inputs['x']),
        'w1': stationary(inputs['L0_conv_w1']),
        'w2': stationary(inputs['L0_conv_w2']),
        'small': _np.concatenate([rows[name] for name in _SMALL], axis=1),
    }

    nc = _bacc.Bacc("TRN2", target_bir_lowering=False, num_devices=1, dynamic_dma_scratch_size=8192)
    arrays, args = {}, {}
    for name, a in given.items():
        arrays[f"{name}_dram"] = a = _np.ascontiguousarray(a)
        args[name] = nc.dram_tensor(f"{name}_dram", a.shape, _mybir.dt.from_np(a.dtype), kind="ExternalInput").ap()
    out = nc.dram_tensor("out_dram", given['x'].shape, _mybir.dt.float32, kind="ExternalOutput").ap()
    bottleneck_kernel(nc, args['x'], args['w1'], args['w2'], args['small'], sizes, out)
    r = _run(nc, [arrays], core_ids=[0])
    return r.results[0]["out_dram"]
```
